# Optimizing a Trainium2 kernel written in Bass

```python
import numpy as np
import jax
import jax.numpy as jnp

def _softmax(x, axis=-1):
    return jax.nn.softmax(x, axis=axis)

def _gelu(x):
    return jax.nn.gelu(x, approximate=True)

def _silu(x):
    return jax.nn.silu(x)

def _sigmoid(x):
    return jax.nn.sigmoid(x)

def _layernorm(x, axis=-1, eps=1e-05):
    m = jnp.mean(x, axis=axis, keepdims=True)
    v = jnp.var(x, axis=axis, keepdims=True)
    return (x - m) / jnp.sqrt(v + eps)

def _scatter_add(tgt, idx, src, axis=0):
    return tgt.at[idx].add(src)

def _segment_sum(src, seg, n):
    return jax.ops.segment_sum(src, seg, n)
kernel_name = 'mk_cond_seq_d2_seqx_r2_f8fa6f'

def setup_inputs(seed: int=0):
    np.random.seed(seed)
    _w = jnp.asarray

    def _rec_inputs():
        import jax
        import jax.numpy as jnp
        _rk = jax.random.key(seed)
        x = -0.0002928 + 1 * jax.random.normal(jax.random.fold_in(_rk, 1), (8, 512, 512), jnp.float32)
        _lenS = 512 - jax.random.randint(jax.random.fold_in(_rk, 7), (8,), 0, max(1, 512 // 4) + 1, jnp.int32)
        _lenS2 = 512 - jax.random.randint(jax.random.fold_in(_rk, 8), (8,), 0, max(1, 512 // 4) + 1, jnp.int32)
        itok_B_0_7 = jax.random.randint(jax.random.fold_in(_rk, 11), (8,), 0, 8, jnp.int32)
        condB_theta = jax.random.uniform(jax.random.fold_in(_rk, 12), (8,), jnp.float32, 0.0, 0.983423)
        condB_phi = jax.random.uniform(jax.random.fold_in(_rk, 13), (8,), jnp.float32, 0.0, 0.961312)
        return (x, itok_B_0_7, condB_theta, condB_phi)
    x, itok_B_0_7, condB_theta, condB_phi = _rec_inputs()

    def _L0_cond_setup():
        import jax, jax.numpy as jnp
        import numpy as np
        E, H, I = (8, 512, 2048)
        B, S = (4, 512)
        LN_EPS = 1e-12
        key = jax.random.key(seed)
        ks = jax.random.split(key, 8)
        x = jax.random.normal(ks[0], (B, S, H), dtype=jnp.float32)
        expert_idx = jax.random.randint(ks[1], (B,), 0, E, dtype=jnp.int64)
        Wi = jax.random.normal(ks[2], (E, H, I), dtype=jnp.float32) * 0.02
        bi = jnp.zeros((E, I), dtype=jnp.float32)
        Wo = jax.random.normal(ks[3], (E, I, H), dtype=jnp.float32) * 0.02
        bo = jnp.zeros((E, H), dtype=jnp.float32)
        gamma = jnp.ones((E, H), dtype=jnp.float32)
        beta = jnp.zeros((E, H), dtype=jnp.float32)
        return {'input_tensor': x, 'expert_idx': expert_idx, 'Wi': Wi, 'bi': bi, 'Wo': Wo, 'bo': bo, 'gamma': gamma, 'beta': beta}
    _L0_cond_all = _L0_cond_setup()
    _L0_cond_in = {k: v for k, v in _L0_cond_all.items() if k in ('Wi', 'bi', 'Wo', 'bo', 'gamma', 'beta')}
    del _L0_cond_all

    def _L1_cond_setup():
        import jax, jax.numpy as jnp
        import numpy as np
        key = jax.random.key(seed)
        k1, k2, k3 = jax.random.split(key, 3)
        B, N, D = (16, 2048, 512)
        embeddings = jax.random.normal(k1, (B, N, D), dtype=jnp.float32)
        theta = jax.random.uniform(k2, (B,), dtype=jnp.float32)
        phi = jax.random.uniform(k3, (B,), dtype=jnp.float32)
        return {'embeddings': embeddings, 'theta': theta, 'phi': phi}
    _L1_cond_all = _L1_cond_setup()
    _L1_cond_in = {k: v for k, v in _L1_cond_all.items() if k in ()}
    del _L1_cond_all
    return {'x': x, 'itok_B_0_7': itok_B_0_7, 'condB_theta': condB_theta, 'condB_phi': condB_phi, 'L0_cond_Wi': _L0_cond_in['Wi'], 'L0_cond_bi': _L0_cond_in['bi'], 'L0_cond_Wo': _L0_cond_in['Wo'], 'L0_cond_bo': _L0_cond_in['bo'], 'L0_cond_gamma': _L0_cond_in['gamma'], 'L0_cond_beta': _L0_cond_in['beta']}

def reference(x, itok_B_0_7, condB_theta, condB_phi, L0_cond_Wi, L0_cond_bi, L0_cond_Wo, L0_cond_bo, L0_cond_gamma, L0_cond_beta):
    import jax
    import jax.numpy as jnp

    def _L0_cond_ref(input_tensor, expert_idx, Wi, bi, Wo, bo, gamma, beta):
        import jax, jax.numpy as jnp
        import numpy as np
        E, H, I = (8, 512, 2048)
        B, S = (4, 512)
        LN_EPS = 1e-12
        Wi_b = Wi[expert_idx]
        bi_b = bi[expert_idx]
        Wo_b = Wo[expert_idx]
        bo_b = bo[expert_idx]
        g_b = gamma[expert_idx]
        be_b = beta[expert_idx]
        h = jax.nn.gelu(jnp.einsum('bsh,bhi->bsi', input_tensor, Wi_b) + bi_b[:, None, :], approximate=False)
        o = jnp.einsum('bsi,bih->bsh', h, Wo_b) + bo_b[:, None, :]
        r = o + input_tensor
        mu = jnp.mean(r, axis=-1, keepdims=True)
        var = jnp.mean(jnp.square(r - mu), axis=-1, keepdims=True)
        y = (r - mu) * jax.lax.rsqrt(var + LN_EPS)
        return y * g_b[:, None, :] + be_b[:, None, :]

    def _L1_cond_ref(embeddings, theta, phi):
        import jax, jax.numpy as jnp
        import numpy as np
        B, N, D = embeddings.shape
        e = embeddings.reshape(B, N, D // 4, 4)
        ct = jnp.cos(theta)[:, None, None]
        st = jnp.sin(theta)[:, None, None]
        cp = jnp.cos(phi)[:, None, None]
        sp = jnp.sin(phi)[:, None, None]
        x0, x1, x2, x3 = (e[..., 0], e[..., 1], e[..., 2], e[..., 3])
        out = jnp.stack([x0 * ct + x1 * st, -x0 * st + x1 * ct, x2 * cp + x3 * sp, -x2 * sp + x3 * cp], axis=-1)
        return out.reshape(B, N, D)
    x = _L0_cond_ref(x, itok_B_0_7, L0_cond_Wi, L0_cond_bi, L0_cond_Wo, L0_cond_bo, L0_cond_gamma, L0_cond_beta)
    x = _L1_cond_ref(x, condB_theta, condB_phi)
    return x

_drawn_inputs = setup_inputs


def setup_inputs(seed=0):
    import zlib

    import numpy as np

    out = dict(_drawn_inputs(seed))
    spreads = {'L0_cond_bi': (0.0, 0.1),
     'L0_cond_bo': (0.0, 0.1),
     'L0_cond_gamma': (1.0, 0.2),
     'L0_cond_beta': (0.0, 0.1)}
    factors = {}
    for name, (base, spread) in spreads.items():
        noise = np.random.default_rng([zlib.crc32(name.encode()), seed]).standard_normal(out[name].shape)
        drawn = base * np.exp(spread * noise) if base else spread * noise
        out[name] = jnp.asarray(drawn.astype(out[name].dtype))
    for name, factor in factors.items():
        out[name] = (out[name] * factor).astype(out[name].dtype)
    return out
```

```python
from contextlib import ExitStack

import numpy as np

import concourse.bass as bass
from concourse import mybir

F32 = mybir.dt.float32
F32R = mybir.dt.float32r
I32 = mybir.dt.int32
ALU = mybir.AluOpType
ACT = mybir.ActivationFunctionType

P = 128
LN_EPS = 1e-12
RING = 4
LAG = 2


def build(nc, xT, x_rows, experts, angles, weights, biases, params, out):
    BATCHES, _, KC, S = xT.shape
    E, TILES, _, TILE_W = weights.shape
    SB = x_rows.shape[2]
    H = x_rows.shape[3]
    WI = KC * P
    EARLY = TILES - LAG
    GROUPS = TILES // RING
    assert TILE_W == WI + H and GROUPS * RING == TILES and H == S == 512

    with ExitStack() as ctx:
        def sb(name, shape, dt):
            return ctx.enter_context(nc.sbuf_tensor(name, shape, dt))

        def sem(name):
            return ctx.enter_context(nc.semaphore(name))

        x_raw = sb("x_raw", [P, KC, S], F32)
        x_high = sb("x_high", [P, KC, S], F32R)
        x_low = sb("x_low", [P, KC, S], F32R)
        x_residual = sb("x_residual", [P, SB, H], F32)
        param = sb("param", [P, 3, H], F32)
        w_raw = sb("w_raw", [P, RING, TILE_W], F32)
        w_high = sb("w_high", [P, RING, TILE_W], F32R)
        w_low = sb("w_low", [P, RING, TILE_W], F32R)
        hidden = sb("hidden", [P, RING, S], F32)
        h_high = sb("h_high", [P, RING, S], F32R)
        h_low = sb("h_low", [P, RING, S], F32R)
        rows = sb("rows", [P, SB, H], F32)
        direct = sb("direct", [P, H], F32)
        crossed = sb("crossed", [P, H], F32)
        result = sb("result", [P, SB, H], F32)
        stats = sb("stats", [P, nc.vector.BN_STATS_DIM], F32)
        moments = sb("moments", [P, SB, nc.vector.BN_AGGR_DIM], F32)
        var_eps = sb("var_eps", [P, 1], F32)
        epsilon = sb("epsilon", [P, 1], F32)
        minus_half = sb("minus_half", [P, 1], F32)
        rstd = sb("rstd", [P, SB], F32)
        gain_direct = sb("gain_direct", [P, H], F32)
        gain_crossed = sb("gain_crossed", [P, H], F32)
        shift = sb("shift", [P, H], F32)
        beta_direct = sb("beta_direct", [P, H], F32)
        beta_crossed = sb("beta_crossed", [P, H], F32)
        expert = sb("expert", [1, BATCHES], I32)
        bias = sb("bias", [P, BATCHES * TILES], F32)
        angle = sb("angle", [P, BATCHES * 2], F32)
        turns = sb("turns", [P, BATCHES * 2], F32)
        whole_turns = sb("whole_turns", [P, BATCHES * 2], I32)
        turned = sb("turned", [P, 4, BATCHES * 2], F32)
        to_cos = sb("to_cos", [P, BATCHES * 2], F32)
        sine = sb("sine", [P, BATCHES * 2], F32)
        cosine = sb("cosine", [P, BATCHES * 2], F32)
        cos4 = sb("cos4", [P, BATCHES, 4], F32)
        sin4 = sb("sin4", [P, BATCHES, 4], F32)

        h_bank = ctx.enter_context(nc.psum_tensor("h_bank", [P, RING, S], F32))
        row_bank = ctx.enter_context(nc.psum_tensor("row_bank", [P, SB, H], F32))

        w_landed = [sem(f"w_landed{i}") for i in range(RING)]
        x_landed = [sem(f"x_landed{k}") for k in range(KC)]
        residual_landed = sem("residual_landed")
        param_landed = sem("param_landed")
        expert_landed = sem("expert_landed")
        bias_landed = sem("bias_landed")
        angle_landed = sem("angle_landed")
        stored = sem("stored")
        x_high_ready = sem("x_high_ready")
        x_split = sem("x_split")
        w_high_ready = sem("w_high_ready")
        w_split = sem("w_split")
        hidden_summed = sem("hidden_summed")
        hidden_ready = sem("hidden_ready")
        h_high_ready = sem("h_high_ready")
        h_split = sem("h_split")
        tile_used = sem("tile_used")
        rows_summed = sem("rows_summed")
        rows_taken = sem("rows_taken")
        residual_ready = sem("residual_ready")
        moments_ready = sem("moments_ready")
        eps_added = sem("eps_added")
        rstd_ready = sem("rstd_ready")
        scaled = sem("scaled")
        rotated = sem("rotated")
        normalized = sem("normalized")
        beta_scaled = sem("beta_scaled")
        tables_ready = sem("tables_ready")
        result_free = sem("result_free")
        trig_step = sem("trig_step")
        angles_ready = sem("angles_ready")
        trig_ready = sem("trig_ready")
        constant_ready = sem("constant_ready")

        def is_first(b):
            return isinstance(b, int) and b == 0

        def pairs(ap):
            return ap.rearrange("p (j two) -> p j two", two=2)

        block = ctx.enter_context(nc.Block())

        @block.sync
        def _(sp):
            def expert_of(b):
                return sp.value_load(expert[0:1, bass.ds(b, 1)], min_val=0, max_val=E - 1)

            def load_tile(e, t, slot):
                sp.dma_start(w_raw[:, slot, :], weights[e, t]).then_inc(w_landed[slot], 16)

            def load_batch(b, last=False):
                e = expert_of(b)
                for t in range(TILES - RING):
                    if t == RING + 1:
                        if not is_first(b):
                            sp.wait_ge(rows_taken, SB * b)
                        sp.dma_start(x_residual[:], x_rows[b]).then_inc(residual_landed, 16)
                        if not is_first(b):
                            sp.wait_ge(tables_ready, b)
                        sp.dma_start(param[:], params[bass.ds(e, 1)].to_broadcast([P, 3, H])) \
                            .then_inc(param_landed, 16)
                    sp.wait_ge(w_split, TILES * b + t + 1)
                    load_tile(e, t + RING, t % RING)
                if last:
                    return
                sp.wait_ge(x_split, KC * (b + 1))
                for k in range(KC):
                    sp.dma_start(x_raw[:, k, :], xT[b + 1][:, k, :]).then_inc(x_landed[k], 16)
                e_next = expert_of(b + 1)
                for slot in range(RING):
                    sp.wait_ge(w_split, TILES * (b + 1) - RING + slot + 1)
                    load_tile(e_next, slot, slot)

            sp.dma_start(expert[:], experts).then_inc(expert_landed, 16)
            sp.wait_ge(expert_landed, 16)
            e_first = expert_of(0)
            for slot in range(RING):
                load_tile(e_first, slot, slot)
            sp.dma_start(angle[:], angles.to_broadcast([P, BATCHES * 2])).then_inc(angle_landed, 16)
            with sp.Fori(0, BATCHES) as b:
                e_b = expert_of(b)
                sp.dma_start(bias[:, bass.ds(b * TILES, TILES)], biases[e_b]).then_inc(bias_landed, 16)
            load_batch(0)
            with sp.Fori(1, BATCHES - 1) as b:
                load_batch(b)
            load_batch(BATCHES - 1, last=True)
            sp.wait_ge(stored, 16 * SB * BATCHES)

        @block.tensor
        def _(pe):
            def three_products(bank, stationary, moving, first, last):
                (s_high, s_low), (m_high, m_low) = stationary, moving
                pe.matmul(bank, s_high, m_high, start=first, stop=False)
                pe.matmul(bank, s_high, m_low, start=False, stop=False)
                return pe.matmul(bank, s_low, m_high, start=False, stop=last)

            def sum_hidden(b, t, slot):
                pe.wait_ge(w_split, TILES * b + t + 1)
                for k in range(KC):
                    if isinstance(t, int) and t == 0:
                        pe.wait_ge(x_split, KC * b + k + 1)
                    cols = slice(k * P, (k + 1) * P)
                    mm = three_products(h_bank[:, slot, :],
                                        (w_high[:, slot, cols], w_low[:, slot, cols]),
                                        (x_high[:, k, :], x_low[:, k, :]), k == 0, k == KC - 1)
                mm.then_inc(hidden_summed, 1)

            def add_share(slot, s, first, last):
                cols = slice(s * P, (s + 1) * P)
                return three_products(row_bank[:, s, :],
                                      (h_high[:, slot, cols], h_low[:, slot, cols]),
                                      (w_high[:, slot, WI:], w_low[:, slot, WI:]), first, last)

            def add_tile(b, t, slot, first=False):
                pe.wait_ge(h_split, TILES * b + t + 1)
                for s in range(SB):
                    if first and not is_first(b):
                        pe.wait_ge(rows_taken, SB * (b - 1) + s + 1)
                    mm = add_share(slot, s, first, False)
                mm.then_inc(tile_used, 1)

            def close_rows(b, s, tiles):
                for t in tiles:
                    pe.wait_ge(h_split, TILES * b + t + 1)
                    mm = add_share(t % RING, s, False, t == TILES - 1)
                mm.then_inc(rows_summed, 1)

            def batch(b, last=False):
                for t in range(LAG):
                    sum_hidden(b, t, t)
                for t in range(LAG, RING):
                    sum_hidden(b, t, t)
                    add_tile(b, t - LAG, t - LAG, first=(t == LAG))
                with pe.Fori(1, GROUPS - 1) as g:
                    for j in range(RING):
                        sum_hidden(b, g * RING + j, j)
                        add_tile(b, g * RING + (j - LAG), (j - LAG) % RING)
                for j in range(RING):
                    t = TILES - RING + j
                    sum_hidden(b, t, j)
                    if t - LAG < TILES - RING or not last:
                        add_tile(b, t - LAG, (j - LAG) % RING)
                if not last:
                    for s in range(SB):
                        close_rows(b, s, range(EARLY, TILES))
                else:
                    pe.wait_ge(h_split, TILES * b + EARLY)
                    for s in range(SB // 2):
                        for t in range(TILES - RING, EARLY):
                            add_share(t % RING, s, False, False)
                    for s in range(SB // 2):
                        close_rows(b, s, range(EARLY, TILES))
                    for s in range(SB // 2, SB):
                        close_rows(b, s, range(TILES - RING, TILES))

            batch(0)
            with pe.Fori(1, BATCHES - 1) as b:
                batch(b)
            batch(BATCHES - 1, last=True)

        @block.scalar
        def _(act):
            def high_x(b):
                for k in range(KC):
                    act.wait_ge(x_landed[k], 16 * (b + 1))
                    act.copy(x_high[:, k, :], x_raw[:, k, :]).then_inc(x_high_ready, 1)

            def high_w(b, group, slot):
                act.wait_ge(w_landed[slot], 16 * (GROUPS * b + group + 1))
                act.copy(w_high[:, slot, :], w_raw[:, slot, :]).then_inc(w_high_ready, 1)

            def activate(b, t, slot):
                act.wait_ge(hidden_summed, TILES * b + t + 1)
                act.activation(hidden[:, slot, :], h_bank[:, slot, :], ACT.Gelu,
                               bias=bias[:, bass.ds(TILES * b + t, 1)]).then_inc(hidden_ready, 1)
                act.wait_ge(hidden_ready, TILES * b + t + 1)
                act.copy(h_high[:, slot, :], hidden[:, slot, :]).then_inc(h_high_ready, 1)

            def step(b, group, j):
                t = group * RING + j
                activate(b, t, j)
                slot = (j + LAG) % RING
                if isinstance(t, int) and t < RING - LAG:
                    if not is_first(b):
                        act.wait_ge(rows_summed, SB * b)
                else:
                    act.wait_ge(tile_used, EARLY * b + t + (LAG - RING + 1))
                high_w(b, group + (j + LAG) // RING, slot)

            def sines():
                act.wait_ge(angles_ready, 1)
                act.activation(sine[:], turned[:, 3, :], ACT.Sin)
                act.activation(cosine[:], to_cos[:], ACT.Sin).then_inc(trig_ready, 1)

            def batch(b, last=False):
                for t in range(RING):
                    step(b, 0, t)
                if is_first(b):
                    sines()
                with act.Fori(1, GROUPS - 1) as g:
                    for j in range(RING):
                        step(b, g, j)
                for j in range(RING - LAG):
                    step(b, GROUPS - 1, j)
                activate(b, TILES - 2, (TILES - 2) % RING)
                if not last:
                    act.wait_ge(tile_used, EARLY * b + EARLY - 1)
                    high_w(b + 1, 0, 0)
                activate(b, TILES - 1, (TILES - 1) % RING)
                if not last:
                    high_x(b + 1)
                    act.wait_ge(tile_used, EARLY * b + EARLY)
                    high_w(b + 1, 0, 1)

            for k in range(KC):
                act.dma_start(x_raw[:, k, :], xT[0][:, k, :]).then_inc(x_landed[k], 16)
            high_x(0)
            high_w(0, 0, 0)
            high_w(0, 0, 1)
            act.wait_ge(bias_landed, 16 * BATCHES)
            batch(0)
            with act.Fori(1, BATCHES - 1) as b:
                batch(b)
            batch(BATCHES - 1, last=True)

        @block.vector
        def _(dve):
            def as_f32(ap):
                return ap.bitcast(F32)

            def low_x(b):
                for k in range(KC):
                    dve.wait_ge(x_high_ready, KC * b + k + 1)
                    dve.tensor_tensor(x_low[:, k, :], x_raw[:, k, :], as_f32(x_high[:, k, :]),
                                      ALU.subtract).then_inc(x_split, 1)

            def low_w(b, t, slot):
                dve.wait_ge(w_high_ready, TILES * b + t + 1)
                dve.tensor_tensor(w_low[:, slot, :], w_raw[:, slot, :], as_f32(w_high[:, slot, :]),
                                  ALU.subtract).then_inc(w_split, 1)

            def low_h(b, t, slot):
                dve.wait_ge(h_high_ready, TILES * b + t + 1)
                dve.tensor_tensor(h_low[:, slot, :], hidden[:, slot, :], as_f32(h_high[:, slot, :]),
                                  ALU.subtract).then_inc(h_split, 1)

            def take_rows(b, s):
                dve.wait_ge(residual_ready, b + 1)
                dve.wait_ge(rows_summed, SB * b + s + 1)
                dve.tensor_tensor(rows[:, s, :], row_bank[:, s, :], x_residual[:, s, :],
                                  ALU.add).then_inc(rows_taken, 1)

            def take_moments(b, s):
                n = SB * b + s + 1
                dve.wait_ge(rows_taken, n)
                dve.bn_stats(stats[:], rows[:, s, :])
                dve.drain()
                dve.bn_aggr(moments[:, s, :], stats[:]).then_inc(moments_ready, 1)

            def scale_rows(b, s):
                dve.wait_ge(moments_ready, SB * b + s + 1)
                dve.wait_ge(tables_ready, b + 1)
                for to, gain in ((direct, gain_direct), (crossed, gain_crossed)):
                    op = dve.scalar_tensor_tensor(out=to[:], in0=rows[:, s, :], scalar=moments[:, s, 0:1],
                                                  in1=gain[:], op0=ALU.subtract, op1=ALU.mult)
                op.then_inc(scaled, 1)

            def rotate_rows(b, s):
                n = SB * b + s + 1
                dve.wait_ge(scaled, n)
                for i in range(2):
                    op = dve.tensor_tensor(pairs(direct[:])[:, :, i], pairs(direct[:])[:, :, i],
                                           pairs(crossed[:])[:, :, 1 - i], ALU.add)
                op.then_inc(rotated, 1)
                dve.wait_ge(rotated, n)
                dve.wait_ge(rstd_ready, n)
                dve.wait_ge(result_free, b + 1)
                dve.scalar_tensor_tensor(out=result[:, s, :], in0=direct[:], scalar=rstd[:, s:s + 1],
                                         in1=shift[:], op0=ALU.mult, op1=ALU.add).then_inc(normalized, 1)

            finish = {0: take_moments, 1: scale_rows, 2: rotate_rows}

            def batch(b, former, last=False):
                if former is not None:
                    for s in range(SB):
                        take_rows(former, s)
                for group in range(GROUPS):
                    for j in range(RING):
                        t = group * RING + j
                        low_h(b, t, j)
                        if t < EARLY:
                            low_w(b, t + LAG, (j + LAG) % RING)
                        if former is not None and j in finish:
                            finish[j](former, group)
                        if t == TILES - 2 and not last:
                            low_w(b + 1, 0, 0)
                if not last:
                    low_x(b + 1)
                    low_w(b + 1, 1, 1)

            low_x(0)
            low_w(0, 0, 0)
            low_w(0, 1, 1)

            two_pi = 2 * np.pi
            part1 = float(np.float32(np.round(two_pi * 2**8) / 2**8))
            part2 = float(np.float32(np.round((two_pi - part1) * 2**20) / 2**20))
            part3 = float(np.float32(two_pi - part1 - part2))
            steps = 0

            def in_turn(op):
                nonlocal steps
                steps += 1
                op.then_inc(trig_step, 1)
                dve.wait_ge(trig_step, steps)

            dve.wait_ge(angle_landed, 16)
            in_turn(dve.tensor_scalar(turns[:], angle[:], float(1 / two_pi), None, ALU.mult))
            in_turn(dve.tensor_copy(whole_turns[:], turns[:]))
            in_turn(dve.tensor_copy(turns[:], whole_turns[:]))
            former_part = angle[:]
            for i, part in enumerate((part1, part2, part3)):
                in_turn(dve.scalar_tensor_tensor(out=turned[:, i, :], in0=turns[:], scalar=-part,
                                                 in1=former_part, op0=ALU.mult, op1=ALU.add))
                former_part = turned[:, i, :]
            pi = float(np.nextafter(np.float32(np.pi), np.float32(0)))
            in_turn(dve.tensor_scalar(turned[:, 3, :], turned[:, 2, :], pi, -pi, ALU.min, ALU.max))
            in_turn(dve.scalar_tensor_tensor(out=to_cos[:], in0=turned[:, 3, :], scalar=-1.0,
                                             in1=turned[:, 3, :], op0=ALU.mult, op1=ALU.max))
            dve.tensor_scalar(to_cos[:], to_cos[:], -1.0, float(np.pi / 2), ALU.mult, ALU.add) \
                .then_inc(angles_ready, 1)

            batch(0, None)
            with dve.Fori(1, BATCHES - 1) as b:
                batch(b, b - 1)
            batch(BATCHES - 1, BATCHES - 2, last=True)
            for s in range(SB):
                take_rows(BATCHES - 1, s)
                for stage in finish.values():
                    stage(BATCHES - 1, s)

        @block.gpsimd
        def _(pool):
            def finish_rows(b, s):
                n = SB * b + s + 1
                pool.wait_ge(moments_ready, n)
                pool.tensor_tensor(var_eps[:], moments[:, s, 1:2], epsilon[:], ALU.add).then_inc(eps_added, 1)
                pool.wait_ge(eps_added, n)
                pool.tensor_tensor(rstd[:, s:s + 1], var_eps[:], minus_half[:], ALU.pow) \
                    .then_inc(rstd_ready, 1)
                pool.wait_ge(normalized, n)
                pool.dma_start(out[b, s], result[:, s, :]).then_inc(stored, 16)

            def add_bias(b):
                pool.wait_ge(param_landed, 16 * (b + 1))
                pool.wait_ge(residual_landed, 16 * (b + 1))
                for s in range(SB):
                    op = pool.tensor_tensor(x_residual[:, s, :], x_residual[:, s, :], param[:, 2, :],
                                            ALU.add)
                op.then_inc(residual_ready, 1)

            def make_tables(b):
                def by_four(ap):
                    return ap.rearrange("p (j four) -> p j four", four=4)

                def turn(four):
                    return four[:, bass.ds(b, 1), :].to_broadcast([P, H // 4, 4])

                for to, which, four in ((beta_direct, 1, cos4), (beta_crossed, 1, sin4),
                                        (gain_direct, 0, cos4), (gain_crossed, 0, sin4)):
                    op = pool.tensor_tensor(by_four(to[:]), by_four(param[:, which, :]), turn(four),
                                            ALU.mult)
                op.then_inc(beta_scaled, 1)
                pool.wait_ge(beta_scaled, b + 1)
                for i in range(2):
                    op = pool.tensor_tensor(pairs(shift[:])[:, :, i], pairs(beta_direct[:])[:, :, i],
                                            pairs(beta_crossed[:])[:, :, 1 - i], ALU.add)
                op.then_inc(tables_ready, 1)

            def batch(b, former):
                if former is not None:
                    for s in range(SB // 2):
                        finish_rows(former, s)
                add_bias(b)
                if former is not None:
                    for s in range(SB // 2, SB):
                        finish_rows(former, s)
                make_tables(b)
                if former is None:
                    pool.sem_inc(result_free, 1)
                else:
                    pool.wait_ge(stored, 16 * SB * (former + 1))
                    pool.sem_inc(result_free, 1)

            pool.memset(epsilon[:], LN_EPS)
            pool.memset(minus_half[:], -0.5).then_inc(constant_ready, 1)
            pool.wait_ge(trig_ready, 1)
            by_angle = lambda ap: ap.rearrange("p b (a two) -> p (b a) two", two=2)
            for i in range(2):
                pool.tensor_copy(by_angle(cos4[:])[:, :, i], cosine[:])
                op = pool.tensor_scalar(by_angle(sin4[:])[:, :, i], sine[:], float(2 * i - 1), None, ALU.mult)
            op.then_inc(constant_ready, 1)
            pool.wait_ge(constant_ready, 2)
            batch(0, None)
            with pool.Fori(1, BATCHES) as b:
                batch(b, b - 1)
            for s in range(SB):
                finish_rows(BATCHES - 1, s)


def kernel(x, itok_B_0_7, condB_theta, condB_phi, L0_cond_Wi, L0_cond_bi, L0_cond_Wo, L0_cond_bo,
           L0_cond_gamma, L0_cond_beta):
    import concourse.bacc as bacc
    from concourse.bass_utils import run_bass_kernel_spmd

    x, Wi, Wo = (np.asarray(a) for a in (x, L0_cond_Wi, L0_cond_Wo))
    B, S, H = x.shape
    E, _, I = Wi.shape
    KC, TILES, SB = H // P, I // P, S // P
    laid = {
        "xT": x.transpose(0, 2, 1).reshape(B, KC, P, S).transpose(0, 2, 1, 3),
        "x_rows": x.reshape(B, SB, P, H).transpose(0, 2, 1, 3),
        "experts": np.asarray(itok_B_0_7).reshape(1, B),
        "angles": np.stack([np.asarray(condB_theta), np.asarray(condB_phi)], 1).reshape(1, 2 * B),
        "weights": np.concatenate([
            Wi.reshape(E, KC, P, TILES, P).transpose(0, 3, 2, 1, 4).reshape(E, TILES, P, KC * P),
            Wo.reshape(E, TILES, P, H)], axis=3),
        "biases": np.asarray(L0_cond_bi).reshape(E, TILES, P).transpose(0, 2, 1),
        "params": np.stack([np.asarray(a) for a in (L0_cond_gamma, L0_cond_beta, L0_cond_bo)], 1),
    }
    nc = bacc.Bacc("TRN2", target_bir_lowering=False, num_devices=1)
    arrays, args = {}, []
    for name, a in laid.items():
        arrays[name + "_dram"] = a = np.ascontiguousarray(a)
        args.append(nc.dram_tensor(name + "_dram", a.shape, mybir.dt.from_np(a.dtype), kind="ExternalInput").ap())
    out = nc.dram_tensor("out_dram", (B, SB, P, H), F32, kind="ExternalOutput").ap()
    build(nc, *args, out)
    result = run_bass_kernel_spmd(nc, [arrays], core_ids=[0])
    return result.results[0]["out_dram"].reshape(B, S, H)
```

```python
from contextlib import ExitStack

import numpy as np

import concourse.bass as bass
from concourse import mybir

F32 = mybir.dt.float32
F32R = mybir.dt.float32r
I32 = mybir.dt.int32
ALU = mybir.AluOpType
ACT = mybir.ActivationFunctionType

P = 128
LN_EPS = 1e-12
RING = 4
LAG = 2


def build(nc, xT, x_rows, experts, angles, weights, biases, params, out):
    BATCHES, _, KC, S = xT.shape
    E, TILES, _, TILE_W = weights.shape
    SB = x_rows.shape[2]
    H = x_rows.shape[3]
    WI = KC * P
    EARLY = TILES - LAG
    GROUPS = TILES // RING
    assert TILE_W == WI + H and GROUPS * RING == TILES and H == S == 512

    with ExitStack() as ctx:
        def sb(name, shape, dt):
            return ctx.enter_context(nc.sbuf_tensor(name, shape, dt))

        def sem(name):
            return ctx.enter_context(nc.semaphore(name))

        x_raw = sb("x_raw", [P, KC, S], F32)
        x_high = sb("x_high", [P, KC, S], F32R)
        x_low = sb("x_low", [P, KC, S], F32R)
        x_residual = sb("x_residual", [P, SB, H], F32)
        param = sb("param", [P, 3, H], F32)
        w_raw = sb("w_raw", [P, RING, TILE_W], F32)
        w_high = sb("w_high", [P, RING, TILE_W], F32R)
        w_low = sb("w_low", [P, RING, TILE_W], F32R)
        hidden = sb("hidden", [P, RING, S], F32)
        h_high = sb("h_high", [P, RING, S], F32R)
        h_low = sb("h_low", [P, RING, S], F32R)
        rows = sb("rows", [P, SB, H], F32)
        direct = sb("direct", [P, H], F32)
        crossed = sb("crossed", [P, H], F32)
        result = sb("result", [P, SB, H], F32)
        stats = sb("stats", [P, nc.vector.BN_STATS_DIM], F32)
        moments = sb("moments", [P, SB, nc.vector.BN_AGGR_DIM], F32)
        var_eps = sb("var_eps", [P, 1], F32)
        epsilon = sb("epsilon", [P, 1], F32)
        minus_half = sb("minus_half", [P, 1], F32)
        rstd = sb("rstd", [P, SB], F32)
        gain_direct = sb("gain_direct", [P, 2, H], F32)
        gain_crossed = sb("gain_crossed", [P, 2, H], F32)
        shift = sb("shift", [P, 2, H], F32)
        beta_direct = sb("beta_direct", [P, H], F32)
        beta_crossed = sb("beta_crossed", [P, H], F32)
        table_loader = sb("table_loader", [P, 1], F32)
        expert = sb("expert", [1, BATCHES], I32)
        bias = sb("bias", [P, E * TILES], F32)
        angle = sb("angle", [P, BATCHES * 2], F32)
        turns = sb("turns", [P, BATCHES * 2], F32)
        whole_turns = sb("whole_turns", [P, BATCHES * 2], I32)
        turned = sb("turned", [P, 4, BATCHES * 2], F32)
        to_cos = sb("to_cos", [P, BATCHES * 2], F32)
        sine = sb("sine", [P, BATCHES * 2], F32)
        cosine = sb("cosine", [P, BATCHES * 2], F32)
        cos4 = sb("cos4", [P, BATCHES, 4], F32)
        sin4 = sb("sin4", [P, BATCHES, 4], F32)

        h_bank = ctx.enter_context(nc.psum_tensor("h_bank", [P, RING, S], F32))
        row_bank = ctx.enter_context(nc.psum_tensor("row_bank", [P, SB, H], F32))

        w_landed = [sem(f"w_landed{i}") for i in range(RING)]
        x_landed = [sem(f"x_landed{k}") for k in range(KC)]
        residual_landed = sem("residual_landed")
        param_landed = sem("param_landed")
        wi_landed = sem("wi_landed")
        expert_landed = sem("expert_landed")
        bias_landed = sem("bias_landed")
        angle_landed = sem("angle_landed")
        stored = sem("stored")
        last_stored = sem("last_stored")
        x_high_ready = sem("x_high_ready")
        x_split = sem("x_split")
        w_high_ready = sem("w_high_ready")
        w_split = sem("w_split")
        wi_high_ready = sem("wi_high_ready")
        wi_split = sem("wi_split")
        hidden_summed = sem("hidden_summed")
        hidden_ready = sem("hidden_ready")
        h_high_ready = sem("h_high_ready")
        h_split = sem("h_split")
        tile_used = sem("tile_used")
        rows_summed = sem("rows_summed")
        rows_taken = sem("rows_taken")
        residual_ready = sem("residual_ready")
        moments_ready = sem("moments_ready")
        eps_added = sem("eps_added")
        rstd_ready = sem("rstd_ready")
        scaled = sem("scaled")
        rotated = sem("rotated")
        normalized = sem("normalized")
        beta_scaled = sem("beta_scaled")
        tables_ready = sem("tables_ready")
        result_free = sem("result_free")
        trig_step = sem("trig_step")
        angles_ready = sem("angles_ready")
        trig_ready = sem("trig_ready")
        constant_ready = sem("constant_ready")

        def copy_of(b):
            return int(isinstance(b, int) and b == BATCHES - 1)

        def is_first(n):
            return isinstance(n, int) and n == 0

        def pairs(ap):
            return ap.rearrange("p (j two) -> p j two", two=2)

        block = ctx.enter_context(nc.Block())

        @block.sync
        def _(sp):
            def expert_of(b):
                return sp.value_load(expert[0:1, bass.ds(b, 1)], min_val=0, max_val=E - 1)

            def load_tile(e, t, slot):
                sp.dma_start(w_raw[:, slot, :], weights[e, t]).then_inc(w_landed[slot], 16)

            def load_batch(b, last=False):
                e = expert_of(b)
                for t in range(TILES - RING):
                    if t == RING + 1:
                        if not is_first(b):
                            sp.wait_ge(rows_taken, SB * b)
                        sp.dma_start(x_residual[:], x_rows[b]).then_inc(residual_landed, 16)
                        if not is_first(b):
                            sp.wait_ge(tables_ready, b)
                        sp.dma_start(param[:], params[bass.ds(e, 1)].to_broadcast([P, 3, H])) \
                            .then_inc(param_landed, 16)
                    sp.wait_ge(w_split, TILES * b + t + 1)
                    load_tile(e, t + RING, t % RING)
                if last:
                    return
                sp.wait_ge(x_split, KC * (b + 1))
                for k in range(KC):
                    sp.dma_start(x_raw[:, k, :], xT[b + 1][:, k, :]).then_inc(x_landed[k], 16)
                e_next = expert_of(b + 1)
                for slot in range(RING):
                    sp.wait_ge(w_split, TILES * (b + 1) - RING + slot + 1)
                    load_tile(e_next, slot, slot)

            sp.dma_start(expert[:], experts).then_inc(expert_landed, 16)
            sp.wait_ge(expert_landed, 16)
            e_first = expert_of(0)
            sp.dma_start(w_raw[:, 0, :WI], weights[e_first, 0][:, :WI]).then_inc(wi_landed, 16)
            sp.dma_start(w_raw[:, 0, WI:], weights[e_first, 0][:, WI:]).then_inc(w_landed[0], 16)
            for slot in range(1, RING):
                load_tile(e_first, slot, slot)
            sp.dma_start(angle[:], angles.to_broadcast([P, BATCHES * 2])).then_inc(angle_landed, 16)
            load_batch(0)
            with sp.Fori(1, BATCHES - 1) as b:
                load_batch(b)
            load_batch(BATCHES - 1, last=True)
            for s in range(SB):
                sp.wait_ge(normalized, SB * (BATCHES - 1) + s + 1)
                sp.dma_start(out[BATCHES - 1, s], result[:, s, :]).then_inc(last_stored, 16)
            sp.wait_ge(stored, 16 * SB * (BATCHES - 1))
            sp.wait_ge(last_stored, 16 * SB)

        @block.tensor
        def _(pe):
            def three_products(bank, stationary, moving, first, last):
                (s_high, s_low), (m_high, m_low) = stationary, moving
                pe.matmul(bank, s_high, m_high, start=first, stop=False)
                pe.matmul(bank, s_high, m_low, start=False, stop=False)
                return pe.matmul(bank, s_low, m_high, start=False, stop=last)

            def sum_hidden(b, t, slot):
                if is_first(b) and is_first(t):
                    pe.wait_ge(wi_split, 1)
                else:
                    pe.wait_ge(w_split, TILES * b + t + 1)
                for k in range(KC):
                    if isinstance(t, int) and t == 0:
                        pe.wait_ge(x_split, KC * b + k + 1)
                    cols = slice(k * P, (k + 1) * P)
                    mm = three_products(h_bank[:, slot, :],
                                        (w_high[:, slot, cols], w_low[:, slot, cols]),
                                        (x_high[:, k, :], x_low[:, k, :]), k == 0, k == KC - 1)
                mm.then_inc(hidden_summed, 1)

            def add_share(slot, s, first, last):
                cols = slice(s * P, (s + 1) * P)
                return three_products(row_bank[:, s, :],
                                      (h_high[:, slot, cols], h_low[:, slot, cols]),
                                      (w_high[:, slot, WI:], w_low[:, slot, WI:]), first, last)

            def add_tile(b, t, slot, first=False):
                pe.wait_ge(h_split, TILES * b + t + 1)
                if is_first(b) and first:
                    pe.wait_ge(w_split, 1)
                for s in range(SB):
                    if first and not is_first(b):
                        pe.wait_ge(rows_taken, SB * (b - 1) + s + 1)
                    mm = add_share(slot, s, first, False)
                mm.then_inc(tile_used, 1)

            def close_rows(b, s, tiles):
                for t in tiles:
                    pe.wait_ge(h_split, TILES * b + t + 1)
                    mm = add_share(t % RING, s, False, t == TILES - 1)
                mm.then_inc(rows_summed, 1)

            def batch(b, last=False):
                for t in range(LAG):
                    sum_hidden(b, t, t)
                for t in range(LAG, RING):
                    sum_hidden(b, t, t)
                    add_tile(b, t - LAG, t - LAG, first=(t == LAG))
                with pe.Fori(1, GROUPS - 1) as g:
                    for j in range(RING):
                        sum_hidden(b, g * RING + j, j)
                        add_tile(b, g * RING + (j - LAG), (j - LAG) % RING)
                for j in range(RING):
                    t = TILES - RING + j
                    sum_hidden(b, t, j)
                    if t - LAG < TILES - RING or not last:
                        add_tile(b, t - LAG, (j - LAG) % RING)
                if not last:
                    for s in range(SB):
                        close_rows(b, s, range(EARLY, TILES))
                else:
                    pe.wait_ge(h_split, TILES * b + EARLY)
                    for s in range(SB // 2):
                        for t in range(TILES - RING, EARLY):
                            add_share(t % RING, s, False, False)
                    for s in range(SB // 2):
                        close_rows(b, s, range(EARLY, TILES))
                    for s in range(SB // 2, SB):
                        close_rows(b, s, range(TILES - RING, TILES))

            batch(0)
            with pe.Fori(1, BATCHES - 1) as b:
                batch(b)
            batch(BATCHES - 1, last=True)

        @block.scalar
        def _(act):
            def high_x(b, chunks=range(KC)):
                for k in chunks:
                    act.wait_ge(x_landed[k], 16 * (b + 1))
                    act.copy(x_high[:, k, :], x_raw[:, k, :]).then_inc(x_high_ready, 1)

            def high_w(b, group, slot):
                act.wait_ge(w_landed[slot], 16 * (GROUPS * b + group + 1))
                act.copy(w_high[:, slot, :], w_raw[:, slot, :]).then_inc(w_high_ready, 1)

            def activate(b, e, t, slot):
                act.wait_ge(hidden_summed, TILES * b + t + 1)
                act.activation(hidden[:, slot, :], h_bank[:, slot, :], ACT.Gelu,
                               bias=bias[:, bass.ds(TILES * e + t, 1)]).then_inc(hidden_ready, 1)
                act.wait_ge(hidden_ready, TILES * b + t + 1)
                act.copy(h_high[:, slot, :], hidden[:, slot, :]).then_inc(h_high_ready, 1)

            def high_ahead(b, group, j):
                t = group * RING + j
                slot = (j + LAG) % RING
                if isinstance(t, int) and t < RING - LAG:
                    if not is_first(b):
                        act.wait_ge(rows_summed, SB * b)
                else:
                    act.wait_ge(tile_used, EARLY * b + t + (LAG - RING + 1))
                high_w(b, group + (j + LAG) // RING, slot)

            def sines():
                act.wait_ge(angles_ready, 1)
                act.activation(sine[:], turned[:, 3, :], ACT.Sin)
                act.activation(cosine[:], to_cos[:], ACT.Sin).then_inc(trig_ready, 1)

            def batch(b, last=False):
                e = act.value_load(expert[0:1, bass.ds(b, 1)], min_val=0, max_val=E - 1)
                for t in range(RING):
                    if t < LAG:
                        high_ahead(b, 0, t)
                    activate(b, e, t, t)
                    if t >= LAG:
                        high_ahead(b, 0, t)
                if is_first(b):
                    sines()
                with act.Fori(1, GROUPS - 1) as g:
                    for j in range(RING):
                        activate(b, e, g * RING + j, j)
                        high_ahead(b, g, j)
                for j in range(RING - LAG):
                    activate(b, e, (GROUPS - 1) * RING + j, j)
                    high_ahead(b, GROUPS - 1, j)
                activate(b, e, TILES - 2, (TILES - 2) % RING)
                if not last:
                    act.wait_ge(tile_used, EARLY * b + EARLY - 1)
                    high_w(b + 1, 0, 0)
                activate(b, e, TILES - 1, (TILES - 1) % RING)
                if not last:
                    high_x(b + 1)
                    act.wait_ge(tile_used, EARLY * b + EARLY)
                    high_w(b + 1, 0, 1)

            for k in range(KC):
                act.dma_start(x_raw[:, k, :], xT[0][:, k, :]).then_inc(x_landed[k], 16)
            act.dma_start(bias[:], biases).then_inc(bias_landed, 16)
            act.wait_ge(constant_ready, 1)
            act.activation(table_loader[:], minus_half[:], ACT.Gelu)
            high_x(0, range(1))
            act.wait_ge(wi_landed, 16)
            act.copy(w_high[:, 0, :WI], w_raw[:, 0, :WI]).then_inc(wi_high_ready, 1)
            high_x(0, range(1, KC))
            act.wait_ge(w_landed[0], 16)
            act.copy(w_high[:, 0, WI:], w_raw[:, 0, WI:]).then_inc(w_high_ready, 1)
            high_w(0, 0, 1)
            act.wait_ge(expert_landed, 16)
            act.wait_ge(bias_landed, 16)
            batch(0)
            with act.Fori(1, BATCHES - 1) as b:
                batch(b)
            batch(BATCHES - 1, last=True)

        @block.vector
        def _(dve):
            def as_f32(ap):
                return ap.bitcast(F32)

            def low_x(b, chunks=range(KC)):
                for k in chunks:
                    dve.wait_ge(x_high_ready, KC * b + k + 1)
                    dve.tensor_tensor(x_low[:, k, :], x_raw[:, k, :], as_f32(x_high[:, k, :]),
                                      ALU.subtract).then_inc(x_split, 1)

            def low_w(b, t, slot):
                dve.wait_ge(w_high_ready, TILES * b + t + 1)
                dve.tensor_tensor(w_low[:, slot, :], w_raw[:, slot, :], as_f32(w_high[:, slot, :]),
                                  ALU.subtract).then_inc(w_split, 1)

            def low_h(b, t, slot):
                dve.wait_ge(h_high_ready, TILES * b + t + 1)
                dve.tensor_tensor(h_low[:, slot, :], hidden[:, slot, :], as_f32(h_high[:, slot, :]),
                                  ALU.subtract).then_inc(h_split, 1)

            def take_rows(b, s):
                dve.wait_ge(residual_ready, b + 1)
                dve.wait_ge(rows_summed, SB * b + s + 1)
                dve.tensor_tensor(rows[:, s, :], row_bank[:, s, :], x_residual[:, s, :],
                                  ALU.add).then_inc(rows_taken, 1)

            def take_moments(b, s):
                n = SB * b + s + 1
                dve.wait_ge(rows_taken, n)
                dve.bn_stats(stats[:], rows[:, s, :])
                dve.drain()
                dve.bn_aggr(moments[:, s, :], stats[:]).then_inc(moments_ready, 1)

            def scale_rows(b, s):
                dve.wait_ge(moments_ready, SB * b + s + 1)
                dve.wait_ge(tables_ready, b + 1)
                for to, gain in ((direct, gain_direct), (crossed, gain_crossed)):
                    op = dve.scalar_tensor_tensor(out=to[:], in0=rows[:, s, :], scalar=moments[:, s, 0:1],
                                                  in1=gain[:, copy_of(b), :], op0=ALU.subtract, op1=ALU.mult)
                op.then_inc(scaled, 1)

            def rotate_rows(b, s):
                n = SB * b + s + 1
                dve.wait_ge(scaled, n)
                for i in range(2):
                    op = dve.tensor_tensor(pairs(direct[:])[:, :, i], pairs(direct[:])[:, :, i],
                                           pairs(crossed[:])[:, :, 1 - i], ALU.add)
                op.then_inc(rotated, 1)
                dve.wait_ge(rotated, n)
                dve.wait_ge(rstd_ready, n)
                dve.wait_ge(result_free, b + 1)
                dve.scalar_tensor_tensor(out=result[:, s, :], in0=direct[:], scalar=rstd[:, s:s + 1],
                                         in1=shift[:, copy_of(b), :], op0=ALU.mult, op1=ALU.add).then_inc(normalized, 1)

            finish = {0: take_moments, 1: scale_rows, 2: rotate_rows}

            def reduce_angles():
                two_pi = 2 * np.pi
                part1 = float(np.float32(np.round(two_pi * 2**8) / 2**8))
                part2 = float(np.float32(np.round((two_pi - part1) * 2**20) / 2**20))
                part3 = float(np.float32(two_pi - part1 - part2))
                steps = 0

                def in_turn(op):
                    nonlocal steps
                    steps += 1
                    op.then_inc(trig_step, 1)
                    dve.wait_ge(trig_step, steps)

                dve.wait_ge(angle_landed, 16)
                in_turn(dve.tensor_scalar(turns[:], angle[:], float(1 / two_pi), None, ALU.mult))
                in_turn(dve.tensor_copy(whole_turns[:], turns[:]))
                in_turn(dve.tensor_copy(turns[:], whole_turns[:]))
                former_part = angle[:]
                for i, part in enumerate((part1, part2, part3)):
                    in_turn(dve.scalar_tensor_tensor(out=turned[:, i, :], in0=turns[:], scalar=-part,
                                                     in1=former_part, op0=ALU.mult, op1=ALU.add))
                    former_part = turned[:, i, :]
                pi = float(np.nextafter(np.float32(np.pi), np.float32(0)))
                in_turn(dve.tensor_scalar(turned[:, 3, :], turned[:, 2, :], pi, -pi, ALU.min, ALU.max))
                in_turn(dve.scalar_tensor_tensor(out=to_cos[:], in0=turned[:, 3, :], scalar=-1.0,
                                                 in1=turned[:, 3, :], op0=ALU.mult, op1=ALU.max))
                dve.tensor_scalar(to_cos[:], to_cos[:], -1.0, float(np.pi / 2), ALU.mult, ALU.add) \
                    .then_inc(angles_ready, 1)

            def batch(b, former, last=False):
                if former is not None:
                    for s in range(SB):
                        take_rows(former, s)
                for group in range(GROUPS):
                    for j in range(RING):
                        t = group * RING + j
                        if t < LAG:
                            low_w(b, t + LAG, (j + LAG) % RING)
                        low_h(b, t, j)
                        if LAG <= t < EARLY:
                            low_w(b, t + LAG, (j + LAG) % RING)
                        if former is not None and j in finish:
                            finish[j](former, group)
                        if is_first(b) and t == LAG:
                            reduce_angles()
                        if t == TILES - 2 and not last:
                            low_w(b + 1, 0, 0)
                if not last:
                    low_x(b + 1)
                    low_w(b + 1, 1, 1)

            low_x(0, range(1))
            dve.wait_ge(wi_high_ready, 1)
            dve.tensor_tensor(w_low[:, 0, :WI], w_raw[:, 0, :WI], as_f32(w_high[:, 0, :WI]),
                              ALU.subtract).then_inc(wi_split, 1)
            low_x(0, range(1, KC))
            dve.wait_ge(w_high_ready, 1)
            dve.tensor_tensor(w_low[:, 0, WI:], w_raw[:, 0, WI:], as_f32(w_high[:, 0, WI:]),
                              ALU.subtract).then_inc(w_split, 1)
            low_w(0, 1, 1)

            batch(0, None)
            with dve.Fori(1, BATCHES - 1) as b:
                batch(b, b - 1)
            batch(BATCHES - 1, BATCHES - 2, last=True)
            for s in range(SB):
                take_rows(BATCHES - 1, s)
                for stage in finish.values():
                    stage(BATCHES - 1, s)

        @block.gpsimd
        def _(pool):
            def finish_rows(b, s):
                n = SB * b + s + 1
                pool.wait_ge(moments_ready, n)
                pool.tensor_tensor(var_eps[:], moments[:, s, 1:2], epsilon[:], ALU.add).then_inc(eps_added, 1)
                pool.wait_ge(eps_added, n)
                pool.tensor_tensor(rstd[:, s:s + 1], var_eps[:], minus_half[:], ALU.pow) \
                    .then_inc(rstd_ready, 1)
                if not copy_of(b):
                    pool.wait_ge(normalized, n)
                    pool.dma_start(out[b, s], result[:, s, :]).then_inc(stored, 16)

            def add_bias(b):
                pool.wait_ge(param_landed, 16 * (b + 1))
                pool.wait_ge(residual_landed, 16 * (b + 1))
                for s in range(SB):
                    op = pool.tensor_tensor(x_residual[:, s, :], x_residual[:, s, :], param[:, 2, :],
                                            ALU.add)
                op.then_inc(residual_ready, 1)

            def make_tables(b):
                def by_four(ap):
                    return ap.rearrange("p (j four) -> p j four", four=4)

                def turn(four):
                    return four[:, bass.ds(b, 1), :].to_broadcast([P, H // 4, 4])

                for to, which, four in ((beta_direct[:], 1, cos4), (beta_crossed[:], 1, sin4),
                                        (gain_direct[:, copy_of(b), :], 0, cos4),
                                        (gain_crossed[:, copy_of(b), :], 0, sin4)):
                    op = pool.tensor_tensor(by_four(to), by_four(param[:, which, :]), turn(four),
                                            ALU.mult)
                op.then_inc(beta_scaled, 1)
                pool.wait_ge(beta_scaled, b + 1)
                for i in range(2):
                    op = pool.tensor_tensor(pairs(shift[:, copy_of(b), :])[:, :, i], pairs(beta_direct[:])[:, :, i],
                                            pairs(beta_crossed[:])[:, :, 1 - i], ALU.add)
                op.then_inc(tables_ready, 1)

            def batch(b, former):
                if former is not None:
                    for s in range(SB // 2):
                        finish_rows(former, s)
                add_bias(b)
                if copy_of(b):
                    make_tables(b)
                if former is not None:
                    for s in range(SB // 2, SB):
                        finish_rows(former, s)
                if not copy_of(b):
                    make_tables(b)
                if former is None:
                    pool.sem_inc(result_free, 1)
                else:
                    pool.wait_ge(stored, 16 * SB * (former + 1))
                    pool.sem_inc(result_free, 1)

            pool.memset(epsilon[:], LN_EPS)
            pool.memset(minus_half[:], -0.5).then_inc(constant_ready, 1)
            pool.wait_ge(trig_ready, 1)
            by_angle = lambda ap: ap.rearrange("p b (a two) -> p (b a) two", two=2)
            for i in range(2):
                pool.tensor_copy(by_angle(cos4[:])[:, :, i], cosine[:])
                op = pool.tensor_scalar(by_angle(sin4[:])[:, :, i], sine[:], float(2 * i - 1), None, ALU.mult)
            op.then_inc(constant_ready, 1)
            pool.wait_ge(constant_ready, 2)
            batch(0, None)
            with pool.Fori(1, BATCHES - 1) as b:
                batch(b, b - 1)
            batch(BATCHES - 1, BATCHES - 2)
            for s in range(SB):
                finish_rows(BATCHES - 1, s)


def kernel(x, itok_B_0_7, condB_theta, condB_phi, L0_cond_Wi, L0_cond_bi, L0_cond_Wo, L0_cond_bo,
           L0_cond_gamma, L0_cond_beta):
    import concourse.bacc as bacc
    from concourse.bass_utils import run_bass_kernel_spmd

    x, Wi, Wo = (np.asarray(a) for a in (x, L0_cond_Wi, L0_cond_Wo))
    B, S, H = x.shape
    E, _, I = Wi.shape
    KC, TILES, SB = H // P, I // P, S // P
    laid = {
        "xT": x.transpose(0, 2, 1).reshape(B, KC, P, S).transpose(0, 2, 1, 3),
        "x_rows": x.reshape(B, SB, P, H).transpose(0, 2, 1, 3),
        "experts": np.asarray(itok_B_0_7).reshape(1, B),
        "angles": np.stack([np.asarray(condB_theta), np.asarray(condB_phi)], 1).reshape(1, 2 * B),
        "weights": np.concatenate([
            Wi.reshape(E, KC, P, TILES, P).transpose(0, 3, 2, 1, 4).reshape(E, TILES, P, KC * P),
            Wo.reshape(E, TILES, P, H)], axis=3),
        "biases": np.asarray(L0_cond_bi).reshape(E * TILES, P).T,
        "params": np.stack([np.asarray(a) for a in (L0_cond_gamma, L0_cond_beta, L0_cond_bo)], 1),
    }
    nc = bacc.Bacc("TRN2", target_bir_lowering=False, num_devices=1)
    arrays, args = {}, []
    for name, a in laid.items():
        arrays[name + "_dram"] = a = np.ascontiguousarray(a)
        args.append(nc.dram_tensor(name + "_dram", a.shape, mybir.dt.from_np(a.dtype), kind="ExternalInput").ap())
    out = nc.dram_tensor("out_dram", (B, SB, P, H), F32, kind="ExternalOutput").ap()
    build(nc, *args, out)
    result = run_bass_kernel_spmd(nc, [arrays], core_ids=[0])
    return result.results[0]["out_dram"].reshape(B, S, H)
```

```python
from contextlib import ExitStack

import numpy as np

import concourse.bass as bass
from concourse import mybir

F32 = mybir.dt.float32
F32R = mybir.dt.float32r
BF16 = mybir.dt.bfloat16
I32 = mybir.dt.int32
ALU = mybir.AluOpType
ACT = mybir.ActivationFunctionType

P = 128
LN_EPS = 1e-12
RING = 4
WARM_UPS = 14
LAG = 2


def build(nc, xT, x_rows, experts, angles, weights, biases, params, out):
    BATCHES, _, KC, S = xT.shape
    E, TILES, _, TILE_W = weights.shape
    SB = x_rows.shape[2]
    H = x_rows.shape[3]
    WI = KC * P
    EARLY = TILES - LAG
    GROUPS = TILES // RING
    assert TILE_W == WI + H and GROUPS * RING == TILES and H == S == 512

    with ExitStack() as ctx:
        def sb(name, shape, dt):
            return ctx.enter_context(nc.sbuf_tensor(name, shape, dt))

        def sem(name):
            return ctx.enter_context(nc.semaphore(name))

        x_raw = sb("x_raw", [P, KC, S], F32)
        x_high = sb("x_high", [P, KC, S], F32R)
        x_low = sb("x_low", [P, KC, S], F32R)
        x_residual = sb("x_residual", [P, SB, H], F32)
        param = sb("param", [P, 3, H], F32)
        w_raw = sb("w_raw", [P, RING, TILE_W], F32)
        w_high = sb("w_high", [P, RING, TILE_W], F32R)
        w_low = sb("w_low", [P, RING, TILE_W], F32R)
        hidden = sb("hidden", [P, RING, S], F32)
        h_high = sb("h_high", [P, RING, S], F32R)
        h_low = sb("h_low", [P, RING, S], F32R)
        rows = sb("rows", [P, SB, H], F32)
        direct = sb("direct", [P, H], F32)
        crossed = sb("crossed", [P, H], F32)
        minus_centred = sb("minus_centred", [P, SB - 1, H], F32)
        minus_crossed = sb("minus_crossed", [P, SB - 1, H], F32)
        turned_rows = sb("turned_rows", [P, SB - 1, H], F32)
        unshifted = sb("unshifted", [P, SB - 1, H], F32)
        result = sb("result", [P, SB, H], F32)
        stats = sb("stats", [P, nc.vector.BN_STATS_DIM], F32)
        moments = sb("moments", [P, SB, nc.vector.BN_AGGR_DIM], F32)
        var_eps = sb("var_eps", [P, SB], F32)
        epsilon = sb("epsilon", [P, 1], F32)
        minus_half = sb("minus_half", [P, 1], F32)
        rstd = sb("rstd", [P, SB], F32)
        gain_direct = sb("gain_direct", [P, 2, H], F32)
        gain_crossed = sb("gain_crossed", [P, 2, H], F32)
        shift = sb("shift", [P, 2, H], F32)
        beta_direct = sb("beta_direct", [P, H], F32)
        beta_crossed = sb("beta_crossed", [P, H], F32)
        zeros = sb("zeros", [P, S], BF16)
        table_loader = sb("table_loader", [P, 1], F32)
        expert = sb("expert", [1, BATCHES], I32)
        bias = sb("bias", [P, E * TILES], F32)
        angle = sb("angle", [P, BATCHES * 2], F32)
        turns = sb("turns", [P, BATCHES * 2], F32)
        whole_turns = sb("whole_turns", [P, BATCHES * 2], I32)
        turned = sb("turned", [P, 4, BATCHES * 2], F32)
        to_cos = sb("to_cos", [P, BATCHES * 2], F32)
        sine = sb("sine", [P, BATCHES * 2], F32)
        cosine = sb("cosine", [P, BATCHES * 2], F32)
        cos4 = sb("cos4", [P, BATCHES, 4], F32)
        sin4 = sb("sin4", [P, BATCHES, 4], F32)

        h_bank = ctx.enter_context(nc.psum_tensor("h_bank", [P, RING, S], F32))
        row_bank = ctx.enter_context(nc.psum_tensor("row_bank", [P, SB, H], F32))

        w_landed = [sem(f"w_landed{i}") for i in range(RING)]
        x_landed = [sem(f"x_landed{k}") for k in range(KC)]
        residual_landed = sem("residual_landed")
        param_landed = sem("param_landed")
        wi_landed = [sem(f"wi_landed{t}") for t in range(LAG)]
        expert_landed = sem("expert_landed")
        bias_landed = sem("bias_landed")
        angle_landed = sem("angle_landed")
        stored = sem("stored")
        last_stored = sem("last_stored")
        x_high_ready = sem("x_high_ready")
        x_split = sem("x_split")
        w_high_ready = sem("w_high_ready")
        w_split = sem("w_split")
        wi_high_ready = sem("wi_high_ready")
        wi_split = sem("wi_split")
        hidden_summed = sem("hidden_summed")
        hidden_ready = sem("hidden_ready")
        h_high_ready = sem("h_high_ready")
        h_split = sem("h_split")
        tile_used = sem("tile_used")
        rows_summed = sem("rows_summed")
        rows_taken = sem("rows_taken")
        residual_ready = sem("residual_ready")
        moments_ready = sem("moments_ready")
        eps_added = sem("eps_added")
        rstd_ready = sem("rstd_ready")
        scaled = sem("scaled")
        rotated = sem("rotated")
        normalized = sem("normalized")
        centred = sem("centred")
        crossed_ready = sem("crossed_ready")
        direct_ready = sem("direct_ready")
        rows_turned = sem("rows_turned")
        rows_scaled = sem("rows_scaled")
        rows_shifted = sem("rows_shifted")
        beta_scaled = sem("beta_scaled")
        tables_ready = sem("tables_ready")
        result_free = sem("result_free")
        trig_step = sem("trig_step")
        angles_ready = sem("angles_ready")
        trig_ready = sem("trig_ready")
        constant_ready = sem("constant_ready")
        zeros_ready = sem("zeros_ready")

        def copy_of(b):
            return int(isinstance(b, int) and b == BATCHES - 1)

        def is_first(n):
            return isinstance(n, int) and n == 0

        def pairs(ap):
            return ap.rearrange("p (j two) -> p j two", two=2)

        block = ctx.enter_context(nc.Block())

        @block.sync
        def _(sp):
            def expert_of(b):
                return sp.value_load(expert[0:1, bass.ds(b, 1)], min_val=0, max_val=E - 1)

            def load_tile(e, t, slot):
                sp.dma_start(w_raw[:, slot, :], weights[e, t]).then_inc(w_landed[slot], 16)

            def load_batch(b, last=False):
                e = expert_of(b)
                for t in range(TILES - RING):
                    if t == RING + 1:
                        if not is_first(b):
                            sp.wait_ge(rows_taken, SB * b)
                        sp.dma_start(x_residual[:], x_rows[b]).then_inc(residual_landed, 16)
                        if not is_first(b):
                            sp.wait_ge(tables_ready, b)
                        sp.dma_start(param[:], params[bass.ds(e, 1)].to_broadcast([P, 3, H])) \
                            .then_inc(param_landed, 16)
                    sp.wait_ge(w_split, TILES * b + t + 1)
                    load_tile(e, t + RING, t % RING)
                if last:
                    return
                sp.wait_ge(x_split, KC * (b + 1))
                for k in range(KC):
                    sp.dma_start(x_raw[:, k, :], xT[b + 1][:, k, :]).then_inc(x_landed[k], 16)
                e_next = expert_of(b + 1)
                for slot in range(RING):
                    sp.wait_ge(w_split, TILES * (b + 1) - RING + slot + 1)
                    load_tile(e_next, slot, slot)

            sp.dma_start(expert[:], experts).then_inc(expert_landed, 16)
            sp.wait_ge(expert_landed, 16)
            e_first = expert_of(0)
            def load_part(t, part, landed):
                sp.dma_start(w_raw[:, t, part], weights[e_first, t][:, part]).then_inc(landed, 16)

            load_part(0, slice(0, WI), wi_landed[0])
            for k in range(KC // 2, KC):
                sp.dma_start(x_raw[:, k, :], xT[0][:, k, :]).then_inc(x_landed[k], 16)
            sp.dma_start(bias[:], biases).then_inc(bias_landed, 16)
            for t in range(1, LAG):
                load_part(t, slice(0, WI), wi_landed[t])
            for t in range(LAG):
                load_part(t, slice(WI, TILE_W), w_landed[t])
            for slot in range(LAG, RING):
                load_tile(e_first, slot, slot)
            sp.dma_start(angle[:], angles.to_broadcast([P, BATCHES * 2])).then_inc(angle_landed, 16)
            load_batch(0)
            with sp.Fori(1, BATCHES - 1) as b:
                load_batch(b)
            load_batch(BATCHES - 1, last=True)
            for s in range(SB):
                if s < SB - 1:
                    sp.wait_ge(rows_shifted, s + 1)
                else:
                    sp.wait_ge(normalized, SB * (BATCHES - 1) + 1)
                sp.dma_start(out[BATCHES - 1, s], result[:, s, :]).then_inc(last_stored, 16)
            sp.wait_ge(stored, 16 * SB * (BATCHES - 1))
            sp.wait_ge(last_stored, 16 * SB)

        @block.tensor
        def _(pe):
            def three_products(bank, stationary, moving, first, last):
                (s_high, s_low), (m_high, m_low) = stationary, moving
                pe.matmul(bank, s_high, m_high, start=first, stop=False)
                pe.matmul(bank, s_high, m_low, start=False, stop=False)
                return pe.matmul(bank, s_low, m_high, start=False, stop=last)

            def sum_hidden(b, t, slot):
                if is_first(b) and isinstance(t, int) and t < LAG:
                    pe.wait_ge(wi_split, t + 1)
                else:
                    pe.wait_ge(w_split, TILES * b + t + 1)
                for k in range(KC):
                    if is_first(t):
                        pe.wait_ge(x_split, KC * b + k + 1)
                    cols = slice(k * P, (k + 1) * P)
                    mm = three_products(h_bank[:, slot, :],
                                        (w_high[:, slot, cols], w_low[:, slot, cols]),
                                        (x_high[:, k, :], x_low[:, k, :]), k == 0, k == KC - 1)
                mm.then_inc(hidden_summed, 1)

            def add_share(slot, s, first, last):
                cols = slice(s * P, (s + 1) * P)
                return three_products(row_bank[:, s, :],
                                      (h_high[:, slot, cols], h_low[:, slot, cols]),
                                      (w_high[:, slot, WI:], w_low[:, slot, WI:]), first, last)

            def add_tile(b, t, slot, first=False):
                pe.wait_ge(h_split, TILES * b + t + 1)
                if is_first(b) and isinstance(t, int) and t < LAG:
                    pe.wait_ge(w_split, t + 1)
                for s in range(SB):
                    if first and not is_first(b):
                        pe.wait_ge(rows_taken, SB * (b - 1) + s + 1)
                    mm = add_share(slot, s, first, False)
                mm.then_inc(tile_used, 1)

            def close_rows(b, s, tiles):
                for t in tiles:
                    pe.wait_ge(h_split, TILES * b + t + 1)
                    mm = add_share(t % RING, s, False, t == TILES - 1)
                mm.then_inc(rows_summed, 1)

            def batch(b, last=False):
                for t in range(LAG):
                    sum_hidden(b, t, t)
                for t in range(LAG, RING):
                    sum_hidden(b, t, t)
                    add_tile(b, t - LAG, t - LAG, first=(t == LAG))
                with pe.Fori(1, GROUPS - 1) as g:
                    for j in range(RING):
                        sum_hidden(b, g * RING + j, j)
                        add_tile(b, g * RING + (j - LAG), (j - LAG) % RING)
                for j in range(RING):
                    t = TILES - RING + j
                    sum_hidden(b, t, j)
                    if t - LAG < TILES - RING or not last:
                        add_tile(b, t - LAG, (j - LAG) % RING)
                if not last:
                    for s in range(SB):
                        close_rows(b, s, range(EARLY, TILES))
                else:
                    pe.wait_ge(h_split, TILES * b + EARLY)
                    for s in range(SB // 2):
                        for t in range(TILES - RING, EARLY):
                            add_share(t % RING, s, False, False)
                    for s in range(SB // 2):
                        close_rows(b, s, range(EARLY, TILES))
                    for s in range(SB // 2, SB):
                        close_rows(b, s, range(TILES - RING, TILES))

            pe.wait_ge(zeros_ready, 1)
            for _ in range(WARM_UPS):
                pe.matmul(h_bank[:, RING - 1, :], zeros[:, :P], zeros[:], start=True, stop=True)
            batch(0)
            with pe.Fori(1, BATCHES - 1) as b:
                batch(b)
            batch(BATCHES - 1, last=True)

        @block.scalar
        def _(act):
            def high_x(b, chunks=range(KC)):
                for k in chunks:
                    act.wait_ge(x_landed[k], 16 * (b + 1))
                    act.copy(x_high[:, k, :], x_raw[:, k, :]).then_inc(x_high_ready, 1)

            def high_w(b, group, slot):
                act.wait_ge(w_landed[slot], 16 * (GROUPS * b + group + 1))
                act.copy(w_high[:, slot, :], w_raw[:, slot, :]).then_inc(w_high_ready, 1)

            def activate(b, e, t, slot):
                act.wait_ge(hidden_summed, TILES * b + t + 1)
                act.activation(hidden[:, slot, :], h_bank[:, slot, :], ACT.Gelu,
                               bias=bias[:, bass.ds(TILES * e + t, 1)]).then_inc(hidden_ready, 1)
                act.wait_ge(hidden_ready, TILES * b + t + 1)
                act.copy(h_high[:, slot, :], hidden[:, slot, :]).then_inc(h_high_ready, 1)

            def high_ahead(b, group, j):
                t = group * RING + j
                slot = (j + LAG) % RING
                if isinstance(t, int) and t < RING - LAG:
                    if not is_first(b):
                        act.wait_ge(rows_summed, SB * b)
                else:
                    act.wait_ge(tile_used, EARLY * b + t + (LAG - RING + 1))
                high_w(b, group + (j + LAG) // RING, slot)

            def sines():
                act.wait_ge(angles_ready, 1)
                act.activation(sine[:], turned[:, 3, :], ACT.Sin)
                act.activation(cosine[:], to_cos[:], ACT.Sin).then_inc(trig_ready, 1)

            def batch(b, last=False):
                e = act.value_load(expert[0:1, bass.ds(b, 1)], min_val=0, max_val=E - 1)
                for t in range(RING):
                    if t < LAG:
                        high_ahead(b, 0, t)
                    activate(b, e, t, t)
                    if t >= LAG:
                        high_ahead(b, 0, t)
                if is_first(b):
                    sines()
                with act.Fori(1, GROUPS - 1) as g:
                    for j in range(RING):
                        activate(b, e, g * RING + j, j)
                        high_ahead(b, g, j)
                for j in range(RING - LAG):
                    activate(b, e, (GROUPS - 1) * RING + j, j)
                    high_ahead(b, GROUPS - 1, j)
                activate(b, e, TILES - 2, (TILES - 2) % RING)
                if not last:
                    act.wait_ge(tile_used, EARLY * b + EARLY - 1)
                    high_w(b + 1, 0, 0)
                activate(b, e, TILES - 1, (TILES - 1) % RING)
                if not last:
                    high_x(b + 1)
                    act.wait_ge(tile_used, EARLY * b + EARLY)
                    high_w(b + 1, 0, 1)

            def high_part(t, part, landed, ready):
                act.wait_ge(landed, 16)
                act.copy(w_high[:, t, part], w_raw[:, t, part]).then_inc(ready, 1)

            for k in range(KC // 2):
                act.dma_start(x_raw[:, k, :], xT[0][:, k, :]).then_inc(x_landed[k], 16)
            act.wait_ge(constant_ready, 1)
            act.activation(table_loader[:], minus_half[:], ACT.Gelu)
            high_x(0, range(1))
            high_part(0, slice(0, WI), wi_landed[0], wi_high_ready)
            high_x(0, range(1, KC))
            for t in range(1, LAG):
                high_part(t, slice(0, WI), wi_landed[t], wi_high_ready)
            for t in range(LAG):
                high_part(t, slice(WI, TILE_W), w_landed[t], w_high_ready)
            act.wait_ge(expert_landed, 16)
            act.wait_ge(bias_landed, 16)
            batch(0)
            with act.Fori(1, BATCHES - 1) as b:
                batch(b)
            batch(BATCHES - 1, last=True)

            def scale_turned(s):
                act.wait_ge(rows_turned, s + 1)
                act.wait_ge(rstd_ready, SB * (BATCHES - 1) + s + 1)
                act.activation(unshifted[:, s, :], turned_rows[:, s, :], ACT.Copy,
                               scale=rstd[:, s:s + 1]).then_inc(rows_scaled, 1)

            for s in range(SB - 1):
                act.wait_ge(moments_ready, SB * (BATCHES - 1) + s + 1)
                act.activation(minus_centred[:, s, :], rows[:, s, :], ACT.Identity,
                               bias=moments[:, s, 0:1], scale=-1.0).then_inc(centred, 1)
                if s > 0:
                    scale_turned(s - 1)
            scale_turned(SB - 2)

        @block.vector
        def _(dve):
            def as_f32(ap):
                return ap.bitcast(F32)

            def low_x(b, chunks=range(KC)):
                for k in chunks:
                    dve.wait_ge(x_high_ready, KC * b + k + 1)
                    dve.tensor_tensor(x_low[:, k, :], x_raw[:, k, :], as_f32(x_high[:, k, :]),
                                      ALU.subtract).then_inc(x_split, 1)

            def low_w(b, t, slot):
                dve.wait_ge(w_high_ready, TILES * b + t + 1)
                dve.tensor_tensor(w_low[:, slot, :], w_raw[:, slot, :], as_f32(w_high[:, slot, :]),
                                  ALU.subtract).then_inc(w_split, 1)

            def low_h(b, t, slot):
                dve.wait_ge(h_high_ready, TILES * b + t + 1)
                dve.tensor_tensor(h_low[:, slot, :], hidden[:, slot, :], as_f32(h_high[:, slot, :]),
                                  ALU.subtract).then_inc(h_split, 1)

            def take_rows(b, s):
                dve.wait_ge(residual_ready, b + 1)
                dve.wait_ge(rows_summed, SB * b + s + 1)
                dve.tensor_tensor(rows[:, s, :], row_bank[:, s, :], x_residual[:, s, :],
                                  ALU.add).then_inc(rows_taken, 1)

            def take_moments(b, s):
                n = SB * b + s + 1
                dve.wait_ge(rows_taken, n)
                dve.bn_stats(stats[:], rows[:, s, :])
                dve.drain()
                dve.bn_aggr(moments[:, s, :], stats[:]).then_inc(moments_ready, 1)

            def scale_rows(b, s):
                dve.wait_ge(moments_ready, SB * b + s + 1)
                dve.wait_ge(tables_ready, b + 1)
                for to, gain in ((direct, gain_direct), (crossed, gain_crossed)):
                    op = dve.scalar_tensor_tensor(out=to[:], in0=rows[:, s, :], scalar=moments[:, s, 0:1],
                                                  in1=gain[:, copy_of(b), :], op0=ALU.subtract, op1=ALU.mult)
                op.then_inc(scaled, 1)

            def rotate_rows(b, s):
                n = SB * b + s + 1
                if copy_of(b):
                    n = SB * b + 1
                dve.wait_ge(scaled, n)
                for i in range(2):
                    op = dve.tensor_tensor(pairs(direct[:])[:, :, i], pairs(direct[:])[:, :, i],
                                           pairs(crossed[:])[:, :, 1 - i], ALU.add)
                op.then_inc(rotated, 1)
                dve.wait_ge(rotated, n)
                dve.wait_ge(rstd_ready, SB * b + s + 1)
                dve.wait_ge(result_free, b + 1)
                dve.scalar_tensor_tensor(out=result[:, s, :], in0=direct[:], scalar=rstd[:, s:s + 1],
                                         in1=shift[:, copy_of(b), :], op0=ALU.mult, op1=ALU.add).then_inc(normalized, 1)

            finish = {0: take_moments, 1: scale_rows, 2: rotate_rows}

            def reduce_angles():
                two_pi = 2 * np.pi
                part1 = float(np.float32(np.round(two_pi * 2**8) / 2**8))
                part2 = float(np.float32(np.round((two_pi - part1) * 2**20) / 2**20))
                part3 = float(np.float32(two_pi - part1 - part2))
                steps = 0

                def in_turn(op):
                    nonlocal steps
                    steps += 1
                    op.then_inc(trig_step, 1)
                    dve.wait_ge(trig_step, steps)

                dve.wait_ge(angle_landed, 16)
                in_turn(dve.tensor_scalar(turns[:], angle[:], float(1 / two_pi), None, ALU.mult))
                in_turn(dve.tensor_copy(whole_turns[:], turns[:]))
                in_turn(dve.tensor_copy(turns[:], whole_turns[:]))
                former_part = angle[:]
                for i, part in enumerate((part1, part2, part3)):
                    in_turn(dve.scalar_tensor_tensor(out=turned[:, i, :], in0=turns[:], scalar=-part,
                                                     in1=former_part, op0=ALU.mult, op1=ALU.add))
                    former_part = turned[:, i, :]
                pi = float(np.nextafter(np.float32(np.pi), np.float32(0)))
                in_turn(dve.tensor_scalar(turned[:, 3, :], turned[:, 2, :], pi, -pi, ALU.min, ALU.max))
                in_turn(dve.scalar_tensor_tensor(out=to_cos[:], in0=turned[:, 3, :], scalar=-1.0,
                                                 in1=turned[:, 3, :], op0=ALU.mult, op1=ALU.max))
                dve.tensor_scalar(to_cos[:], to_cos[:], -1.0, float(np.pi / 2), ALU.mult, ALU.add) \
                    .then_inc(angles_ready, 1)

            def batch(b, former, last=False):
                if former is not None:
                    for s in range(SB):
                        take_rows(former, s)
                for group in range(GROUPS):
                    for j in range(RING):
                        t = group * RING + j
                        if t < LAG:
                            low_w(b, t + LAG, (j + LAG) % RING)
                        low_h(b, t, j)
                        if LAG <= t < EARLY:
                            low_w(b, t + LAG, (j + LAG) % RING)
                        if former is not None and j in finish:
                            finish[j](former, group)
                        if is_first(b) and t == LAG:
                            reduce_angles()
                        if t == TILES - 2 and not last:
                            low_w(b + 1, 0, 0)
                if not last:
                    low_x(b + 1)
                    low_w(b + 1, 1, 1)

            def low_part(t, part, high_ready, split):
                dve.wait_ge(high_ready, t + 1)
                dve.tensor_tensor(w_low[:, t, part], w_raw[:, t, part], as_f32(w_high[:, t, part]),
                                  ALU.subtract).then_inc(split, 1)

            dve.memset(zeros[:], 0.0).then_inc(zeros_ready, 1)
            low_x(0, range(1))
            low_part(0, slice(0, WI), wi_high_ready, wi_split)
            low_x(0, range(1, KC))
            for t in range(1, LAG):
                low_part(t, slice(0, WI), wi_high_ready, wi_split)
            for t in range(LAG):
                low_part(t, slice(WI, TILE_W), w_high_ready, w_split)

            batch(0, None)
            with dve.Fori(1, BATCHES - 1) as b:
                batch(b, b - 1)
            batch(BATCHES - 1, BATCHES - 2, last=True)

            def turn_shared(s):
                dve.wait_ge(crossed_ready, s + 1)
                dve.wait_ge(direct_ready, s + 1)
                for i in range(2):
                    op = dve.tensor_tensor(pairs(turned_rows[:, s, :])[:, :, i],
                                           pairs(turned_rows[:, s, :])[:, :, i],
                                           pairs(minus_crossed[:, s, :])[:, :, 1 - i], ALU.subtract)
                op.then_inc(rows_turned, 1)

            b = BATCHES - 1
            for s in range(SB - 1):
                take_rows(b, s)
                take_moments(b, s)
                dve.wait_ge(moments_ready, SB * b + s + 1)
                if s == 0:
                    dve.wait_ge(tables_ready, b + 1)
                dve.scalar_tensor_tensor(out=turned_rows[:, s, :], in0=rows[:, s, :],
                                         scalar=moments[:, s, 0:1], in1=gain_direct[:, copy_of(b), :],
                                         op0=ALU.subtract, op1=ALU.mult).then_inc(direct_ready, 1)
                if s > 0:
                    turn_shared(s - 1)
            take_rows(b, SB - 1)
            take_moments(b, SB - 1)
            turn_shared(SB - 2)
            scale_rows(b, SB - 1)
            rotate_rows(b, SB - 1)

        @block.gpsimd
        def _(pool):
            def make_rstd(b, s):
                n = SB * b + s + 1
                pool.wait_ge(moments_ready, n)
                pool.tensor_tensor(var_eps[:, s:s + 1], moments[:, s, 1:2], epsilon[:], ALU.add).then_inc(eps_added, 1)
                pool.wait_ge(eps_added, n)
                pool.tensor_tensor(rstd[:, s:s + 1], var_eps[:, s:s + 1], minus_half[:], ALU.pow) \
                    .then_inc(rstd_ready, 1)

            def finish_rows(b, s):
                make_rstd(b, s)
                pool.wait_ge(normalized, SB * b + s + 1)
                pool.dma_start(out[b, s], result[:, s, :]).then_inc(stored, 16)

            def add_bias(b):
                pool.wait_ge(param_landed, 16 * (b + 1))
                pool.wait_ge(residual_landed, 16 * (b + 1))
                for s in range(SB):
                    op = pool.tensor_tensor(x_residual[:, s, :], x_residual[:, s, :], param[:, 2, :],
                                            ALU.add)
                op.then_inc(residual_ready, 1)

            def make_tables(b):
                def by_four(ap):
                    return ap.rearrange("p (j four) -> p j four", four=4)

                def turn(four):
                    return four[:, bass.ds(b, 1), :].to_broadcast([P, H // 4, 4])

                for to, which, four in ((beta_direct[:], 1, cos4), (beta_crossed[:], 1, sin4),
                                        (gain_direct[:, copy_of(b), :], 0, cos4),
                                        (gain_crossed[:, copy_of(b), :], 0, sin4)):
                    op = pool.tensor_tensor(by_four(to), by_four(param[:, which, :]), turn(four),
                                            ALU.mult)
                op.then_inc(beta_scaled, 1)
                pool.wait_ge(beta_scaled, b + 1)
                for i in range(2):
                    op = pool.tensor_tensor(pairs(shift[:, copy_of(b), :])[:, :, i], pairs(beta_direct[:])[:, :, i],
                                            pairs(beta_crossed[:])[:, :, 1 - i], ALU.add)
                op.then_inc(tables_ready, 1)

            def batch(b, former):
                if former is not None:
                    for s in range(SB // 2):
                        finish_rows(former, s)
                add_bias(b)
                if copy_of(b):
                    make_tables(b)
                if former is not None:
                    for s in range(SB // 2, SB):
                        finish_rows(former, s)
                if not copy_of(b):
                    make_tables(b)
                if former is None:
                    pool.sem_inc(result_free, 1)
                else:
                    pool.wait_ge(stored, 16 * SB * (former + 1))
                    pool.sem_inc(result_free, 1)

            pool.memset(epsilon[:], LN_EPS)
            pool.memset(minus_half[:], -0.5).then_inc(constant_ready, 1)
            pool.wait_ge(trig_ready, 1)
            by_angle = lambda ap: ap.rearrange("p b (a two) -> p (b a) two", two=2)
            for i in range(2):
                pool.tensor_copy(by_angle(cos4[:])[:, :, i], cosine[:])
                op = pool.tensor_scalar(by_angle(sin4[:])[:, :, i], sine[:], float(2 * i - 1), None, ALU.mult)
            op.then_inc(constant_ready, 1)
            pool.wait_ge(constant_ready, 2)
            batch(0, None)
            with pool.Fori(1, BATCHES - 1) as b:
                batch(b, b - 1)
            batch(BATCHES - 1, BATCHES - 2)

            def shift_shared(s):
                pool.wait_ge(rows_scaled, s + 1)
                pool.tensor_tensor(result[:, s, :], unshifted[:, s, :], shift[:, copy_of(BATCHES - 1), :],
                                   ALU.add).then_inc(rows_shifted, 1)

            for s in range(SB - 1):
                make_rstd(BATCHES - 1, s)
                pool.wait_ge(centred, s + 1)
                pool.tensor_tensor(minus_crossed[:, s, :], minus_centred[:, s, :],
                                   gain_crossed[:, copy_of(BATCHES - 1), :], ALU.mult).then_inc(crossed_ready, 1)
                if s > 0:
                    shift_shared(s - 1)
            make_rstd(BATCHES - 1, SB - 1)
            shift_shared(SB - 2)


def kernel(x, itok_B_0_7, condB_theta, condB_phi, L0_cond_Wi, L0_cond_bi, L0_cond_Wo, L0_cond_bo,
           L0_cond_gamma, L0_cond_beta):
    import concourse.bacc as bacc
    from concourse.bass_utils import run_bass_kernel_spmd

    x, Wi, Wo = (np.asarray(a) for a in (x, L0_cond_Wi, L0_cond_Wo))
    B, S, H = x.shape
    E, _, I = Wi.shape
    KC, TILES, SB = H // P, I // P, S // P
    laid = {
        "xT": x.transpose(0, 2, 1).reshape(B, KC, P, S).transpose(0, 2, 1, 3),
        "x_rows": x.reshape(B, SB, P, H).transpose(0, 2, 1, 3),
        "experts": np.asarray(itok_B_0_7).reshape(1, B),
        "angles": np.stack([np.asarray(condB_theta), np.asarray(condB_phi)], 1).reshape(1, 2 * B),
        "weights": np.concatenate([
            Wi.reshape(E, KC, P, TILES, P).transpose(0, 3, 2, 1, 4).reshape(E, TILES, P, KC * P),
            Wo.reshape(E, TILES, P, H)], axis=3),
        "biases": np.asarray(L0_cond_bi).reshape(E * TILES, P).T,
        "params": np.stack([np.asarray(a) for a in (L0_cond_gamma, L0_cond_beta, L0_cond_bo)], 1),
    }
    nc = bacc.Bacc("TRN2", target_bir_lowering=False, num_devices=1)
    arrays, args = {}, []
    for name, a in laid.items():
        arrays[name + "_dram"] = a = np.ascontiguousarray(a)
        args.append(nc.dram_tensor(name + "_dram", a.shape, mybir.dt.from_np(a.dtype), kind="ExternalInput").ap())
    out = nc.dram_tensor("out_dram", (B, SB, P, H), F32, kind="ExternalOutput").ap()
    build(nc, *args, out)
    result = run_bass_kernel_spmd(nc, [arrays], core_ids=[0])
    return result.results[0]["out_dram"].reshape(B, S, H)
```
